# Optimizing a Trainium2 kernel written in Bass

```python
import numpy as np
import jax
import jax.numpy as jnp

def _softmax(x, axis=-1):
    return jax.nn.softmax(x, axis=axis)

def _gelu(x):
    return jax.nn.gelu(x, approximate=True)

def _silu(x):
    return jax.nn.silu(x)

def _sigmoid(x):
    return jax.nn.sigmoid(x)

def _layernorm(x, axis=-1, eps=1e-05):
    m = jnp.mean(x, axis=axis, keepdims=True)
    v = jnp.var(x, axis=axis, keepdims=True)
    return (x - m) / jnp.sqrt(v + eps)

def _scatter_add(tgt, idx, src, axis=0):
    return tgt.at[idx].add(src)

def _segment_sum(src, seg, n):
    return jax.ops.segment_sum(src, seg, n)
kernel_name = 'mk_cond_resid_d4_seqx_r4_bd901b'

def setup_inputs(seed: int=0):
    np.random.seed(seed)
    _w = jnp.asarray

    def _rec_inputs():
        import jax
        import jax.numpy as jnp
        _rk = jax.random.key(seed)
        x = -0.000125 + 0.9999 * jax.random.normal(jax.random.fold_in(_rk, 1), (8, 256, 1024), jnp.float32)
        _lenS = 256 - jax.random.randint(jax.random.fold_in(_rk, 7), (8,), 0, max(1, 256 // 4) + 1, jnp.int32)
        _lenS2 = 256 - jax.random.randint(jax.random.fold_in(_rk, 8), (8,), 0, max(1, 256 // 4) + 1, jnp.int32)
        itok_B_3_7 = jax.random.randint(jax.random.fold_in(_rk, 11), (8,), 3, 8, jnp.int32)
        itok_B_0_23 = jax.random.randint(jax.random.fold_in(_rk, 12), (8,), 0, 24, jnp.int32)
        condB_coeff = 0.00219231 + 0.0100837 * jax.random.normal(jax.random.fold_in(_rk, 13), (8,), jnp.float32)
        itok_B_6_15 = jax.random.randint(jax.random.fold_in(_rk, 15), (8,), 6, 16, jnp.int32)
        _validS = jnp.arange(256)[None, :] < _lenS[:, None]
        _validS2 = jnp.arange(256)[None, :] < _lenS2[:, None]
        _causal = jnp.tril(jnp.ones((256, 256), dtype=bool))
        mask_Bx4096x4096_ik1 = jnp.where(jnp.ones((8, 1024, 1024), dtype=bool), 1, 0).astype(jnp.int32)
        return (x, itok_B_3_7, itok_B_0_23, condB_coeff, itok_B_6_15, mask_Bx4096x4096_ik1)
    x, itok_B_3_7, itok_B_0_23, condB_coeff, itok_B_6_15, mask_Bx4096x4096_ik1 = _rec_inputs()

    def _L0_cond_setup():
        import jax, jax.numpy as jnp
        import numpy as np
        MAX_LORAS, OUT, IN = (8, 1024, 1024)
        B, S = (4, 512)
        key = jax.random.key(seed)
        k1, k2, k3 = jax.random.split(key, 3)
        x = jax.random.normal(k1, (B, S, IN), dtype=jnp.float32)
        weight = jax.random.normal(k2, (MAX_LORAS, OUT, IN), dtype=jnp.float32) * 0.02
        adapter_ids = jax.random.randint(k3, (B,), 0, MAX_LORAS, dtype=jnp.int32)
        return {'x': x, 'weight': weight, 'adapter_ids': adapter_ids}
    _L0_cond_all = _L0_cond_setup()
    _L0_cond_in = {k: v for k, v in _L0_cond_all.items() if k in ('weight',)}
    del _L0_cond_all

    def _L1_cond_setup():
        import jax, jax.numpy as jnp
        import numpy as np
        R = 16
        ALPHA = 32
        SCALING = ALPHA / R
        SLOTS = 32
        IN_F = 1024
        OUT_F = 1024
        B, T = (8, 256)
        key = jax.random.key(seed)
        k1, k2, k3, k4, k5, k6 = jax.random.split(key, 6)
        x = jax.random.normal(k1, (B, T, IN_F), dtype=jnp.float32)
        adapter_mapping = jax.random.randint(k2, (B,), 0, SLOTS, dtype=jnp.int32)
        W = jax.random.normal(k3, (OUT_F, IN_F), dtype=jnp.float32) * 0.02
        b = jax.random.normal(k4, (OUT_F,), dtype=jnp.float32) * 0.02
        lora_As = jax.random.normal(k5, (SLOTS, IN_F, R), dtype=jnp.float32) * 0.02
        lora_Bs = jax.random.normal(k6, (SLOTS, R, OUT_F), dtype=jnp.float32) * 0.02
        return {'x': x, 'adapter_mapping': adapter_mapping, 'W': W, 'b': b, 'lora_As': lora_As, 'lora_Bs': lora_Bs}
    _L1_cond_all = _L1_cond_setup()
    _L1_cond_in = {k: v for k, v in _L1_cond_all.items() if k in ('W', 'b', 'lora_As', 'lora_Bs')}
    del _L1_cond_all

    def _L2_cond_setup():
        import jax, jax.numpy as jnp
        import numpy as np
        B, S, D_IN, D_OUT = (4, 128, 1024, 1024)
        key = jax.random.key(seed)
        k1, k2, k3, k4, k5 = jax.random.split(key, 5)
        hidden_states = jax.random.normal(k1, (B, S, D_IN), dtype=jnp.float32)
        W = jax.random.normal(k2, (D_OUT, D_IN), dtype=jnp.float32) * 0.02
        b = jax.random.normal(k3, (D_OUT,), dtype=jnp.float32) * 0.02
        coeff = jax.random.normal(k4, (B,), dtype=jnp.float32) * 0.01
        mask = jax.random.randint(k5, (B, D_IN, D_OUT), 0, 2, dtype=jnp.int32)
        return {'hidden_states': hidden_states, 'W': W, 'b': b, 'coeff': coeff, 'mask': mask}
    _L2_cond_all = _L2_cond_setup()
    _L2_cond_in = {k: v for k, v in _L2_cond_all.items() if k in ('W', 'b')}
    del _L2_cond_all

    def _L3_cond_setup():
        import jax, jax.numpy as jnp
        import numpy as np
        B, S, D_IN, D_OUT = (4, 512, 1024, 1024)
        RANK, MAX_LORAS = (16, 32)
        key = jax.random.key(seed)
        ks = jax.random.split(key, 6)
        x = jax.random.normal(ks[0], (B, S, D_IN), dtype=jnp.float32)
        adapter_ids = jax.random.randint(ks[1], (B,), 0, MAX_LORAS)
        base_weight = jax.random.normal(ks[2], (D_OUT, D_IN), dtype=jnp.float32) * D_IN ** (-0.5)
        base_bias = jax.random.normal(ks[3], (D_OUT,), dtype=jnp.float32) * 0.01
        lora_A_w = jax.random.normal(ks[4], (MAX_LORAS, RANK, D_IN), dtype=jnp.float32) * D_IN ** (-0.5)
        lora_B_w = jax.random.normal(ks[5], (MAX_LORAS, D_OUT, RANK), dtype=jnp.float32) * RANK ** (-0.5)
        return {'x': x, 'adapter_ids': adapter_ids, 'base_weight': base_weight, 'base_bias': base_bias, 'lora_A_w': lora_A_w, 'lora_B_w': lora_B_w}
    _L3_cond_all = _L3_cond_setup()
    _L3_cond_in = {k: v for k, v in _L3_cond_all.items() if k in ('base_weight', 'base_bias', 'lora_A_w', 'lora_B_w')}
    del _L3_cond_all
    return {'x': x, 'itok_B_3_7': itok_B_3_7, 'itok_B_0_23': itok_B_0_23, 'condB_coeff': condB_coeff, 'itok_B_6_15': itok_B_6_15, 'mask_Bx4096x4096_ik1': mask_Bx4096x4096_ik1, 'L0_cond_weight': _L0_cond_in['weight'], 'L1_cond_W': _L1_cond_in['W'], 'L1_cond_b': _L1_cond_in['b'], 'L1_cond_lora_As': _L1_cond_in['lora_As'], 'L1_cond_lora_Bs': _L1_cond_in['lora_Bs'], 'L2_cond_W': _L2_cond_in['W'], 'L2_cond_b': _L2_cond_in['b'], 'L3_cond_base_weight': _L3_cond_in['base_weight'], 'L3_cond_base_bias': _L3_cond_in['base_bias'], 'L3_cond_lora_A_w': _L3_cond_in['lora_A_w'], 'L3_cond_lora_B_w': _L3_cond_in['lora_B_w']}

def reference(x, itok_B_3_7, itok_B_0_23, condB_coeff, itok_B_6_15, mask_Bx4096x4096_ik1, L0_cond_weight, L1_cond_W, L1_cond_b, L1_cond_lora_As, L1_cond_lora_Bs, L2_cond_W, L2_cond_b, L3_cond_base_weight, L3_cond_base_bias, L3_cond_lora_A_w, L3_cond_lora_B_w):
    import jax
    import jax.numpy as jnp

    def _L0_cond_ref(x, weight, adapter_ids):
        import jax, jax.numpy as jnp
        import numpy as np
        MAX_LORAS, OUT, IN = (8, 1024, 1024)
        B, S = (4, 512)
        w = weight[adapter_ids]
        return jnp.einsum('bsi,boi->bso', x, w)

    def _L1_cond_ref(x, adapter_mapping, W, b, lora_As, lora_Bs):
        import jax, jax.numpy as jnp
        import numpy as np
        R = 16
        ALPHA = 32
        SCALING = ALPHA / R
        SLOTS = 32
        IN_F = 1024
        OUT_F = 1024
        B, T = (8, 256)
        base_out = jnp.einsum('bti,oi->bto', x, W) + b
        A = lora_As[adapter_mapping]
        Bm = lora_Bs[adapter_mapping]
        lora_h = jnp.einsum('bti,bir->btr', x, A)
        lora_out = jnp.einsum('btr,bro->bto', lora_h, Bm)
        return base_out + lora_out * SCALING

    def _L2_cond_ref(hidden_states, W, b, coeff, mask):
        import jax, jax.numpy as jnp
        import numpy as np
        B, S, D_IN, D_OUT = (4, 128, 1024, 1024)
        output = jnp.einsum('bsi,oi->bso', hidden_states, W) + b
        sign = (2 * mask - 1).astype(hidden_states.dtype)
        diff = jnp.einsum('bsi,bio->bso', hidden_states, sign)
        return output + diff * coeff[:, None, None]

    def _L3_cond_ref(x, adapter_ids, base_weight, base_bias, lora_A_w, lora_B_w):
        import jax, jax.numpy as jnp
        import numpy as np
        B, S, D_IN, D_OUT = (4, 512, 1024, 1024)
        RANK, MAX_LORAS = (16, 32)
        result = jnp.einsum('bsd,od->bso', x, base_weight) + base_bias
        A = lora_A_w[adapter_ids]
        Bw = lora_B_w[adapter_ids]
        h = jnp.einsum('bsd,brd->bsr', x, A)
        lora_out = jnp.einsum('bsr,bor->bso', h, Bw)
        result = result + lora_out
        return result.astype(x.dtype)
    x = x + _L0_cond_ref(x, L0_cond_weight, itok_B_3_7)
    x = x + _L1_cond_ref(x, itok_B_0_23, L1_cond_W, L1_cond_b, L1_cond_lora_As, L1_cond_lora_Bs)
    x = x + _L2_cond_ref(x, L2_cond_W, L2_cond_b, condB_coeff, mask_Bx4096x4096_ik1)
    x = x + _L3_cond_ref(x, itok_B_6_15, L3_cond_base_weight, L3_cond_base_bias, L3_cond_lora_A_w, L3_cond_lora_B_w)
    return x

_drawn_inputs = setup_inputs


def setup_inputs(seed=0):
    import zlib

    import numpy as np

    out = dict(_drawn_inputs(seed))
    spreads = {}
    factors = {'L1_cond_b': 5.281, 'L2_cond_b': 5.38, 'L3_cond_base_bias': 8.0}
    for name, (base, spread) in spreads.items():
        noise = np.random.default_rng([zlib.crc32(name.encode()), seed]).standard_normal(out[name].shape)
        drawn = base * np.exp(spread * noise) if base else spread * noise
        out[name] = jnp.asarray(drawn.astype(out[name].dtype))
    for name, factor in factors.items():
        out[name] = (out[name] * factor).astype(out[name].dtype)
    return out
```

```python
from contextlib import ExitStack

import concourse.bass as bass
from concourse import mybir

F32 = mybir.dt.float32
F32R = mybir.dt.float32r
I32 = mybir.dt.int32
ALU = mybir.AluOpType
ACT = mybir.ActivationFunctionType

P = 128
BATCHES, TOKENS, D = 8, 256, 1024
PAIR = 2
PAIRS = BATCHES // PAIR
N = PAIR * TOKENS
KT = D // P
OT = D // P
RANK = 16
STACK = P // (2 * RANK)
UNIT = KT * P
RING = 4
LAYERS = 4
PHASES = PAIRS * LAYERS // 2
OWN_UNITS = OT * PAIR
PHASE_UNITS = OWN_UNITS + OT
PAIR_UNITS = 2 * PHASE_UNITS
PHASE_TILES = 2 * OT
PAIR_TILES = LAYERS * OT
PAIR_GROUPS = PAIR_UNITS // RING
OWN_GROUPS = OWN_UNITS // RING
STAGE = 4
LORA_SCALE = {1: 2.0, 3: 1.0}
OWN_BANKS = 2
SHARED_BANK = [2, 3, 4, 5, 6, 0, 1, 2]
LORA_BANK = 7
DRAINED0 = OWN_BANKS
LORA_AFTER = 3


def build(nc, x, ids, coeff, w0, w1, w2, w3, mask, b1, b2, b3, a1, a3, lb1, lb3, out):
    with ExitStack() as ctx:
        def sb(name, shape, dt):
            return ctx.enter_context(nc.sbuf_tensor(name, shape, dt))

        def sem(name):
            return ctx.enter_context(nc.semaphore(name))

        act_hi = [sb(f"act_hi{s}", [P, KT * N], F32R) for s in range(2)]
        act_lo = [sb(f"act_lo{s}", [P, KT * N], F32R) for s in range(2)]
        resid = sb("resid", [P, OT * N], F32)
        stage = sb("stage", [P, STAGE * N], F32)
        w2_sb = sb("w2_sb", [P, OT * UNIT], F32)
        raw = sb("raw", [P, RING * UNIT], F32)
        raw_mask = raw[:, :].bitcast(I32)
        w_hi = sb("w_hi", [P, RING * UNIT], F32R)
        w_lo = sb("w_lo", [P, RING * UNIT], F32R)
        merged = sb("merged", [P, 2 * UNIT], F32)
        lora_a_raw = sb("lora_a_raw", [P, PAIR * KT * RANK], F32)
        lora_b_raw = sb("lora_b_raw", [P, PAIR * D], F32)
        lora_a = sb("lora_a", [P, PAIR * KT * P], F32R)
        lora_b = sb("lora_b", [P, PAIR * D], F32R)
        lora_h = sb("lora_h", [P, N], F32R)
        bias = sb("bias", [P, 3 * OT], F32)
        coeff_sb = sb("coeff_sb", [P, BATCHES], F32)
        pair_ids = sb("pair_ids", [1, 3 * PAIR], I32)
        banks = [ctx.enter_context(nc.psum_tensor(f"bank{i}", [P, N], F32)) for i in range(8)]

        ids_loaded = sem("ids_loaded")
        consts_loaded = sem("consts_loaded")
        raw_loaded = [sem(f"raw_loaded{s}") for s in range(RING)]
        stage_loaded = [sem(f"stage_loaded{s}") for s in range(STAGE)]
        first_loaded = [sem(f"first_loaded{k}") for k in range(KT)]
        w2_loaded = sem("w2_loaded")
        lora_loaded = sem("lora_loaded")
        w_hi_ready = sem("w_hi_ready")
        w_ready = sem("w_ready")
        units_done = sem("units_done")
        sign_ready = sem("sign_ready")
        merged_ready = sem("merged_ready")
        tile_done = sem("tile_done")
        tile_drained = sem("tile_drained")
        half_sum = sem("half_sum")
        act_hi_ready = sem("act_hi_ready")
        act_ready = sem("act_ready")
        lora_hi_ready = sem("lora_hi_ready")
        lora_ready = sem("lora_ready")
        h_summed = sem("h_summed")
        h_hi_ready = sem("h_hi_ready")
        h_ready = sem("h_ready")
        stored = sem("stored")
        results_stored = sem("results_stored")
        ids_seen = sem("ids_seen")
        pair_entered = sem("pair_entered")
        block = ctx.enter_context(nc.Block())

        def tile(buf, o):
            return buf[:, bass.ds(o * N, N)]

        def slot(buf, s):
            return buf[:, s * UNIT:(s + 1) * UNIT]

        def stacked(b):
            return lora_a[:, b * KT * P:(b + 1) * KT * P].rearrange("p (k g r) -> p k g r", k=KT, g=STACK)

        def plain_a(b):
            return lora_a_raw[:, b * KT * RANK:(b + 1) * KT * RANK].rearrange(
                "p (k r) -> p k r", k=KT).unsqueeze(2).broadcast_to([P, KT, STACK, RANK])

        @block.sync
        def _(sp):
            def after_split(p, u):
                sp.wait_ge(w_ready, PAIR_UNITS * p + u + 1)

            def after_merge(p, u):
                sp.wait_ge(merged_ready, OWN_UNITS * p + u - RING - PHASE_UNITS + 1)

            def load_group(p, g, base, buf, free, src_of):
                for j in range(RING):
                    free(p, base + RING * g + j)
                    sp.dma_start(slot(buf, j), src_of(j)).then_inc(raw_loaded[j], 16)

            def pick(table, i):
                return table[bass.ds(i, 1), :, :].rearrange("a p n -> (a p) n")

            def load_lora(p, half, a_ids, a_table, b_table):
                sp.wait_ge(lora_ready, 2 * p + half + 1)
                for b in range(PAIR):
                    sp.dma_start(lora_a_raw[:, b * KT * RANK:(b + 1) * KT * RANK],
                                 pick(a_table, a_ids[b])).then_inc(lora_loaded, 16)
                    for g in range(2 * STACK):
                        sp.dma_start(lora_b_raw[g * RANK:(g + 1) * RANK, b * D:(b + 1) * D],
                                     pick(b_table, a_ids[b])).then_inc(lora_loaded, 16)

            def load_pair(p, last):
                sp.dma_start(pair_ids[:, :], ids[bass.ds(p, 1), :]).then_inc(ids_loaded, 16)
                sp.wait_ge(ids_loaded, 16 * (p + 1))
                sp.sem_inc(ids_seen, 1)
                rows = [sp.value_load(pair_ids[0:1, j:j + 1], min_val=0, max_val=m - 1)
                        for j, m in enumerate([8, 8, 32, 32, 32, 32])]
                with sp.Fori(0, OWN_GROUPS) as g:
                    load_group(p, g, 0, raw, after_split,
                               lambda j: pick(w0, rows[j % 2] * OT + 2 * g + j // 2))
                load_lora(p, 0, rows[2:4], a1, lb1)
                with sp.Fori(0, OT // RING) as g:
                    load_group(p, g, OWN_UNITS, raw, after_split, lambda j: pick(w1, RING * g + j))

                def mask_unit(g):
                    return lambda j: pick(mask, (PAIR * p + j % 2) * OT + 2 * g + j // 2)

                load_group(p, 0, PHASE_UNITS, raw_mask, after_split, mask_unit(0))
                with sp.Fori(1, OWN_GROUPS) as g:
                    load_group(p, g, PHASE_UNITS, raw_mask, after_merge, mask_unit(g))
                load_lora(p, 1, rows[4:6], a3, lb3)
                for g, free in ((0, after_merge), (1, after_split)):
                    load_group(p, g, PHASE_UNITS + OWN_UNITS, raw, free,
                               lambda j: w3[RING * g + j, :, :])
                if not last:
                    for k in range(KT):
                        sp.wait_ge(act_ready, PAIR_TILES * p + k + STAGE + 1 + (PAIR_TILES - KT) * (k >= STAGE))
                        sp.dma_start(tile(stage, k % STAGE), pick(x, (p + 1) * KT + k)).then_inc(
                            stage_loaded[k % STAGE], 16)

            with sp.Fori(0, PAIRS - 1) as p:
                load_pair(p, False)
            load_pair(PAIRS - 1, True)

        @block.gpsimd
        def _(pool):
            pool.sem_inc(results_stored, 1)
            for o in range(OT):
                pool.wait_ge(w_ready, OWN_UNITS + o + 1)
                pool.dma_start(slot(w2_sb, o), w2[o, :, :]).then_inc(w2_loaded, 16)
            with pool.Fori(0, PAIRS) as p:
                with pool.Fori(0, OT) as o:
                    pool.wait_ge(tile_drained, PAIR_TILES * p + o + DRAINED0 + 3 * OT + 1)
                    pool.dma_start(out[bass.ds(p * OT + o, 1), :, :].rearrange("a p n -> (a p) n"),
                                   tile(resid, o)).then_inc(stored, 16)
                pool.wait_ge(stored, 16 * OT * p + 16 * OT)
                pool.sem_inc(results_stored, 1)
            pool.wait_ge(stored, 16 * OT * PAIRS)

        @block.scalar
        def _(act):
            def weight_hi(p, u, s):
                act.wait_ge(raw_loaded[s], 16 * (PAIR_GROUPS * p + 1) + 16 // RING * (u - s))
                act.wait_ge(units_done, PAIR_UNITS * p + u + 1)
                nc.scalar.activation(slot(w_hi, s), slot(raw, s), ACT.Copy).then_inc(w_hi_ready, 1)

            def sign(p, u, s):
                act.wait_ge(raw_loaded[s], 16 * (PAIR_GROUPS * p + 1) + 16 // RING * (u - s))
                act.wait_ge(w_ready, PAIR_UNITS * p + u - 1 + RING)
                nc.scalar.activation(slot(merged, s % 2), slot(raw_mask, s), ACT.Copy,
                                     scale=2.0, bias=-1.0).then_inc(sign_ready, 1)

            def merged_hi(p, u, s):
                act.wait_ge(merged_ready, OWN_UNITS * p + u - PHASE_UNITS + 1)
                act.wait_ge(units_done, PAIR_UNITS * p + u + 1)
                nc.scalar.activation(slot(w_hi, s), slot(merged, s % 2), ACT.Copy).then_inc(w_hi_ready, 1)

            def result_hi(p, layer, o):
                act.wait_ge(tile_drained, PAIR_TILES * p + layer * OT + o + DRAINED0 + 1)
                nc.scalar.activation(tile(act_hi[(layer + 1) % 2], o), tile(resid, o),
                                     ACT.Copy).then_inc(act_hi_ready, 1)

            def first_hi(k):
                act.wait_ge(first_loaded[k], 16)
                nc.scalar.activation(tile(act_hi[0], k), tile(resid, k), ACT.Copy).then_inc(act_hi_ready, 1)

            def next_input_hi(p, k):
                act.wait_ge(stage_loaded[k % STAGE], 16 * (KT // STAGE * p + k // STAGE + 1))
                nc.scalar.activation(tile(act_hi[0], k), tile(stage, k % STAGE), ACT.Copy).then_inc(act_hi_ready, 1)

            def lora_hi(p, half, scale):
                act.wait_ge(lora_loaded, 16 * PAIR * (1 + 2 * STACK) * (2 * p + half + 1))
                for b in range(PAIR):
                    nc.scalar.activation(stacked(b)[:, :, :, 0:RANK], plain_a(b), ACT.Copy)
                    nc.scalar.activation(lora_b[:, b * D:(b + 1) * D], lora_b_raw[:, b * D:(b + 1) * D],
                                         ACT.Copy, scale=scale).then_inc(lora_hi_ready, 1)

            def own_layer(p, layer, unit_steps):
                base = PHASE_UNITS * (layer // 2)
                with act.Fori(0, OWN_GROUPS - 1) as g:
                    for j in range(2):
                        unit_steps(p, base + RING * g + RING + 2 * j, 2 * j)
                        result_hi(p, layer, 2 * g + j)
                for j in range(2):
                    u = base + OWN_UNITS + 2 * j
                    weight_hi(p, u, 2 * j)
                    result_hi(p, layer, OT - 2 + j)
                    weight_hi(p, u + 1, 2 * j + 1)

            def plain_steps(p, u, s):
                weight_hi(p, u, s)
                weight_hi(p, u + 1, s + 1)

            def mask_steps(p, u, s):
                sign(p, u, s)
                sign(p, u + 1, s + 1)
                merged_hi(p, u, s)
                merged_hi(p, u + 1, s + 1)

            def shared_layer(p, layer, last):
                base = PHASE_UNITS * (layer // 2) + OWN_UNITS
                half = layer // 2
                lora_hi(p, half, LORA_SCALE[layer])
                for o in range(RING):
                    if o == LORA_AFTER:
                        act.wait_ge(h_summed, 2 * p + half + 1)
                        nc.scalar.activation(lora_h[:, :], banks[LORA_BANK][:, :], ACT.Copy).then_inc(h_hi_ready, 1)
                    weight_hi(p, base + RING + o, o)
                    if layer == 3 and not last:
                        next_input_hi(p, o)
                if layer == 1:
                    for o in range(RING):
                        result_hi(p, layer, o)
                for o in range(RING, OT):
                    if layer == 1:
                        u = PHASE_UNITS + o - RING
                        sign(p, u, o % RING)
                        result_hi(p, layer, o)
                        merged_hi(p, u, o % RING)
                    elif not last:
                        next_input_hi(p, o)
                        weight_hi(p + 1, o - RING, o % RING)

            def pair(p, last):
                own_layer(p, 0, plain_steps)
                shared_layer(p, 1, last)
                own_layer(p, 2, mask_steps)
                shared_layer(p, 3, last)

            for k in range(KT):
                act.dma_start(tile(resid, k), x[k, :, :]).then_inc(first_loaded[k], 16)
            act.dma_start(coeff_sb[:, :], coeff).then_inc(consts_loaded, 16)
            for n, b in enumerate((b1, b2, b3)):
                act.dma_start(bias[:, n * OT:(n + 1) * OT], b).then_inc(consts_loaded, 16)
            first_hi(0)
            weight_hi(0, 0, 0)
            for k in range(1, KT):
                first_hi(k)
            for u in range(1, RING):
                weight_hi(0, u, u)
            with act.Fori(0, PAIRS - 1) as p:
                pair(p, False)
            pair(PAIRS - 1, True)

        @block.vector
        def _(dve):
            def minus_hi(dst, src):
                return nc.vector.tensor_tensor(dst, src[0], src[1], ALU.subtract)

            def weight_lo(p, u, s):
                dve.wait_ge(w_hi_ready, PAIR_UNITS * p + u + 1)
                minus_hi(slot(w_lo, s), (slot(raw, s), slot(w_hi, s).bitcast(F32))).then_inc(w_ready, 1)

            def merge(p, u, s, o, b):
                dve.wait_ge(sign_ready, OWN_UNITS * p + u - PHASE_UNITS + 1)
                nc.vector.scalar_tensor_tensor(
                    slot(merged, s % 2), slot(merged, s % 2), coeff_sb[:, bass.ds(PAIR * p + b, 1)],
                    w2_sb[:, bass.ds(o * UNIT, UNIT)], ALU.mult, ALU.add).then_inc(merged_ready, 1)

            def merged_lo(p, u, s):
                dve.wait_ge(w_hi_ready, PAIR_UNITS * p + u + 1)
                minus_hi(slot(w_lo, s), (slot(merged, s % 2), slot(w_hi, s).bitcast(F32))).then_inc(w_ready, 1)

            def sum_tile(p, layer, o, bank):
                if layer % 2:
                    dve.wait_ge(tile_done, PHASE_TILES * p + layer // 2 * OT + o + 1)
                else:
                    dve.wait_ge(units_done, RING + PAIR_UNITS * p + layer // 2 * PHASE_UNITS + PAIR * (o + 1))
                if layer == 0:
                    nc.vector.tensor_tensor(tile(resid, o), banks[bank][:, :], tile(act_hi[0], o).bitcast(F32),
                                            ALU.add).then_inc(half_sum, 1)
                    dve.wait_ge(half_sum, OT * p + o + 1)
                    nc.vector.tensor_tensor(tile(resid, o), tile(resid, o), tile(act_lo[0], o).bitcast(F32),
                                            ALU.add).then_inc(tile_drained, 1)
                else:
                    nc.vector.scalar_tensor_tensor(
                        tile(resid, o), banks[bank][:, :], bias[:, bass.ds((layer - 1) * OT + o, 1)],
                        tile(resid, o), ALU.add, ALU.add).then_inc(tile_drained, 1)

            def result_lo(p, layer, o):
                dve.wait_ge(act_hi_ready, PAIR_TILES * p + (layer + 1) * OT + o + 1)
                s = (layer + 1) % 2
                minus_hi(tile(act_lo[s], o),
                         (tile(resid, o), tile(act_hi[s], o).bitcast(F32))).then_inc(act_ready, 1)

            def input_lo(p, k, src):
                dve.wait_ge(act_hi_ready, PAIR_TILES * p + k + 1)
                minus_hi(tile(act_lo[0], k), (src, tile(act_hi[0], k).bitcast(F32))).then_inc(act_ready, 1)

            def lora_lo(p, half, scale):
                for b in range(PAIR):
                    dve.wait_ge(lora_hi_ready, PAIR * (2 * p + half) + b + 1)
                    hi = stacked(b)[:, :, :, 0:RANK].bitcast(F32)
                    minus_hi(stacked(b)[:, :, :, RANK:2 * RANK], (plain_a(b), hi))
                    low = lora_b[P // 2:P, b * D:(b + 1) * D]
                    last = nc.vector.scalar_tensor_tensor(low, lora_b_raw[P // 2:P, b * D:(b + 1) * D], scale,
                                                          low.bitcast(F32), ALU.mult, ALU.subtract)
                last.then_inc(lora_ready, 1)

            def h_lo(p, half):
                dve.wait_ge(h_hi_ready, 2 * p + half + 1)
                for q in (P // 4, 3 * P // 4):
                    rows = slice(q, q + P // 4)
                    last = nc.vector.tensor_tensor(lora_h[rows, :], banks[LORA_BANK][rows, :],
                                                   lora_h[rows, :].bitcast(F32), ALU.subtract)
                last.then_inc(h_ready, 1)

            def own_layer(p, layer):
                base = PHASE_UNITS * (layer // 2)
                with dve.Fori(0, OWN_GROUPS - 1) as g:
                    for j in range(2):
                        u = base + RING * g + RING + 2 * j
                        if layer == 2:
                            merge(p, u, 2 * j, 2 * g + 2 + j, 0)
                            merge(p, u + 1, 2 * j + 1, 2 * g + 2 + j, 1)
                            merged_lo(p, u, 2 * j)
                        else:
                            weight_lo(p, u, 2 * j)
                        sum_tile(p, layer, 2 * g + j, j)
                        if layer == 2:
                            merged_lo(p, u + 1, 2 * j + 1)
                        else:
                            weight_lo(p, u + 1, 2 * j + 1)
                        result_lo(p, layer, 2 * g + j)
                for j in range(2):
                    u = base + OWN_UNITS + 2 * j
                    weight_lo(p, u, 2 * j)
                    sum_tile(p, layer, OT - 2 + j, j)
                    result_lo(p, layer, OT - 2 + j)
                    weight_lo(p, u + 1, 2 * j + 1)

            def shared_layer(p, layer, last):
                base = PHASE_UNITS * (layer // 2) + OWN_UNITS
                half = layer // 2
                lora_lo(p, half, LORA_SCALE[layer])
                for o in range(RING):
                    if o == LORA_AFTER:
                        h_lo(p, half)
                    weight_lo(p, base + RING + o, o)
                    if layer == 3 and not last:
                        input_lo(p + 1, o, tile(stage, o))
                for o in range(RING):
                    sum_tile(p, layer, o, SHARED_BANK[o])
                    if layer == 1 and o:
                        result_lo(p, layer, o - 1)
                if layer == 1:
                    result_lo(p, layer, RING - 1)
                    dve.wait_ge(w2_loaded, 16 * OT)
                for o in range(RING, OT):
                    if layer == 1:
                        u = PHASE_UNITS + o - RING
                        merge(p, u, o % RING, (o - RING) // 2, o % 2)
                        sum_tile(p, layer, o, SHARED_BANK[o])
                        result_lo(p, layer, o)
                        merged_lo(p, u, o % RING)
                    else:
                        if not last:
                            input_lo(p + 1, o, tile(stage, o % STAGE))
                        sum_tile(p, layer, o, SHARED_BANK[o])
                        if not last:
                            weight_lo(p + 1, o - RING, o % RING)

            def pair(p, last):
                dve.wait_ge(results_stored, p + 1)
                dve.sem_inc(pair_entered, 1)
                dve.wait_ge(consts_loaded, 4 * 16)
                own_layer(p, 0)
                shared_layer(p, 1, last)
                own_layer(p, 2)
                shared_layer(p, 3, last)

            dve.sem_inc(w_ready, RING)
            dve.sem_inc(tile_drained, DRAINED0)
            dve.sem_inc(lora_ready, 1)
            input_lo(0, 0, tile(resid, 0))
            weight_lo(0, 0, 0)
            for k in range(1, KT):
                input_lo(0, k, tile(resid, k))
            for u in range(1, RING):
                weight_lo(0, u, u)
            with dve.Fori(0, PAIRS - 1) as p:
                pair(p, False)
            pair(PAIRS - 1, True)

        @block.tensor
        def _(pe):
            def unit(s, out_ap, cols, src, k_wait, opened):
                for k in range(KT):
                    if k_wait is not None:
                        pe.wait_ge(act_ready, k_wait + k + 1)
                    hi = w_hi[:, s * UNIT + k * P:s * UNIT + (k + 1) * P]
                    lo = w_lo[:, s * UNIT + k * P:s * UNIT + (k + 1) * P]
                    x_hi = act_hi[src][:, k * N + cols[0]:k * N + cols[1]]
                    x_lo = act_lo[src][:, k * N + cols[0]:k * N + cols[1]]
                    nc.tensor.matmul(out_ap, hi, x_hi, start=(k == 0), stop=False)
                    nc.tensor.matmul(out_ap, hi, x_lo, start=False, stop=False)
                    last = nc.tensor.matmul(out_ap, lo, x_hi, start=False, stop=(k == KT - 1 and not opened))
                last.then_inc(units_done, 1)

            def own_group(f, g, first):
                for j in range(2):
                    pe.wait_ge(tile_drained, PHASE_TILES * f + 2 * g + j + 1)
                    for b in range(PAIR):
                        s = 2 * j + b
                        pe.wait_ge(w_ready, RING + PHASE_UNITS * f + RING * g + s + 1)
                        cols = (b * TOKENS, (b + 1) * TOKENS)
                        unit(s, banks[j][:, cols[0]:cols[1]], cols, 0,
                             PHASE_TILES * f if first and s == 0 else None, False)

            def low_rank(f):
                pe.wait_ge(lora_ready, f + 2)
                for b in range(PAIR):
                    cols = slice(b * TOKENS, (b + 1) * TOKENS)
                    for k in range(KT):
                        a = lora_a[:, (b * KT + k) * P:(b * KT + k + 1) * P]
                        for i, part in enumerate((act_hi[1], act_lo[1])):
                            last = nc.tensor.matmul(
                                banks[LORA_BANK][:, cols], a,
                                part[:, k * N + b * TOKENS:k * N + (b + 1) * TOKENS],
                                start=(k == 0 and i == 0), stop=(k == KT - 1 and i == 1))
                last.then_inc(h_summed, 1)

            def low_rank_out(o):
                for b in range(PAIR):
                    cols = slice(b * TOKENS, (b + 1) * TOKENS)
                    last = nc.tensor.matmul(banks[SHARED_BANK[o]][:, cols],
                                            lora_b[:, b * D + o * P:b * D + (o + 1) * P], lora_h[:, cols],
                                            start=False, stop=(b == PAIR - 1))
                last.then_inc(tile_done, 1)

            pe.sem_inc(units_done, RING)
            with pe.Fori(0, PHASES) as f:
                own_group(f, 0, True)
                with pe.Fori(1, OWN_GROUPS) as g:
                    own_group(f, g, False)
                for o in range(OT):
                    if o == LORA_AFTER:
                        low_rank(f)
                    if SHARED_BANK[o] < OWN_BANKS or o == OT - 1:
                        before = OT - OWN_BANKS + SHARED_BANK[o] if o < OT - 1 else OT
                        pe.wait_ge(tile_drained, PHASE_TILES * f + before + DRAINED0 + 1)
                    pe.wait_ge(w_ready, RING + PHASE_UNITS * f + OWN_UNITS + o + 1)
                    unit(o % RING, banks[SHARED_BANK[o]][:, :], (0, N), 1,
                         PHASE_TILES * f + OT if o == 0 else None, True)
                    if o == LORA_AFTER:
                        pe.wait_ge(h_ready, f + 1)
                        for done in range(o):
                            low_rank_out(done)
                    if o >= LORA_AFTER:
                        low_rank_out(o)


def kernel(x, itok_B_3_7, itok_B_0_23, condB_coeff, itok_B_6_15, mask_Bx4096x4096_ik1, L0_cond_weight,
           L1_cond_W, L1_cond_b, L1_cond_lora_As, L1_cond_lora_Bs, L2_cond_W, L2_cond_b,
           L3_cond_base_weight, L3_cond_base_bias, L3_cond_lora_A_w, L3_cond_lora_B_w):
    import numpy as np
    import concourse.bacc as bacc
    from concourse.bass_utils import run_bass_kernel_spmd as run

    def units(w):
        w = np.asarray(w).reshape(-1, OT, P, KT, P)
        return np.ascontiguousarray(w.transpose(0, 1, 4, 3, 2)).reshape(-1, P, UNIT)

    m = np.asarray(mask_Bx4096x4096_ik1).reshape(BATCHES, KT, P, OT, P)
    ids = np.stack([np.asarray(i).reshape(PAIRS, PAIR) for i in (itok_B_3_7, itok_B_0_23, itok_B_6_15)], axis=1)
    a3 = np.asarray(L3_cond_lora_A_w)
    arrays = {
        "x": np.asarray(x).reshape(PAIRS, PAIR, TOKENS, KT, P).transpose(0, 3, 4, 1, 2).reshape(PAIRS * KT, P, N),
        "ids": ids.reshape(PAIRS, 3 * PAIR),
        "coeff": np.asarray(condB_coeff).reshape(1, BATCHES),
        "w0": units(L0_cond_weight),
        "w1": units(L1_cond_W),
        "w2": units(L2_cond_W),
        "w3": units(L3_cond_base_weight),
        "mask": m.transpose(0, 3, 2, 1, 4).reshape(BATCHES * OT, P, UNIT),
        "b1": np.asarray(L1_cond_b).reshape(OT, P).T,
        "b2": np.asarray(L2_cond_b).reshape(OT, P).T,
        "b3": np.asarray(L3_cond_base_bias).reshape(OT, P).T,
        "a1": np.asarray(L1_cond_lora_As).reshape(-1, KT, P, RANK).transpose(0, 2, 1, 3).reshape(-1, P, KT * RANK),
        "a3": a3.reshape(-1, RANK, KT, P).transpose(0, 3, 2, 1).reshape(-1, P, KT * RANK),
        "lb1": np.asarray(L1_cond_lora_Bs),
        "lb3": np.asarray(L3_cond_lora_B_w).transpose(0, 2, 1),
    }
    arrays = {f"{k}_dram": np.ascontiguousarray(v) for k, v in arrays.items()}
    nc = bacc.Bacc("TRN2", target_bir_lowering=False, num_devices=1)
    args = {k[:-5]: nc.dram_tensor(k, v.shape, mybir.dt.from_np(v.dtype), kind="ExternalInput").ap()
            for k, v in arrays.items()}
    args["coeff"] = args["coeff"].broadcast_to([P, BATCHES])
    out = nc.dram_tensor("out_dram", (PAIRS * OT, P, N), F32, kind="ExternalOutput").ap()
    build(nc, out=out, **args)
    r = run(nc, [arrays], core_ids=[0])
    y = np.asarray(r.results[0]["out_dram"]).reshape(PAIRS, OT, P, PAIR, TOKENS)
    return y.transpose(0, 3, 4, 1, 2).reshape(BATCHES, TOKENS, D)
```

```python
from contextlib import ExitStack

import concourse.bass as bass
from concourse import mybir

F32 = mybir.dt.float32
F32R = mybir.dt.float32r
I32 = mybir.dt.int32
ALU = mybir.AluOpType
ACT = mybir.ActivationFunctionType

P = 128
BATCHES, TOKENS, D = 8, 256, 1024
PAIR = 2
PAIRS = BATCHES // PAIR
N = PAIR * TOKENS
KT = D // P
OT = D // P
RANK = 16
STACK = P // (2 * RANK)
UNIT = KT * P
RING = 4
LAYERS = 4
PHASES = PAIRS * LAYERS // 2
OWN_UNITS = OT * PAIR
PHASE_UNITS = OWN_UNITS + OT
PAIR_UNITS = 2 * PHASE_UNITS
PHASE_TILES = 2 * OT
PAIR_TILES = LAYERS * OT
PAIR_GROUPS = PAIR_UNITS // RING
OWN_GROUPS = OWN_UNITS // RING
STAGE = 4
LORA_SCALE = {1: 2.0, 3: 1.0}
OWN_BANKS = 2
SHARED_BANK = [2, 3, 4, 5, 6, 0, 1, 2]
LORA_BANK = 7
DRAINED0 = OWN_BANKS
LORA_AFTER = 3
FIRST_AT_ONCE = 5
FIRST_SPLIT = 5


def build(nc, x, ids, coeff, w0, w1, w2, w3, mask, b1, b2, b3, a1, a3, lb1, lb3, out):
    with ExitStack() as ctx:
        def sb(name, shape, dt):
            return ctx.enter_context(nc.sbuf_tensor(name, shape, dt))

        def sem(name):
            return ctx.enter_context(nc.semaphore(name))

        act_hi = [sb(f"act_hi{s}", [P, KT * N], F32R) for s in range(2)]
        act_lo = [sb(f"act_lo{s}", [P, KT * N], F32R) for s in range(2)]
        resid = sb("resid", [P, OT * N], F32)
        w2_sb = sb("w2_sb", [P, OT * UNIT], F32)
        raw = sb("raw", [P, RING * UNIT], F32)
        raw_mask = raw[:, :].bitcast(I32)
        w_hi = sb("w_hi", [P, RING * UNIT], F32R)
        w_lo = sb("w_lo", [P, RING * UNIT], F32R)
        merged = sb("merged", [P, RING * UNIT], F32)
        stage = merged
        lora_a_raw = sb("lora_a_raw", [P, PAIR * KT * RANK], F32)
        lora_b_raw = sb("lora_b_raw", [P, PAIR * D], F32)
        lora_a = sb("lora_a", [P, PAIR * KT * P], F32R)
        lora_b = sb("lora_b", [P, PAIR * D], F32R)
        lora_h = sb("lora_h", [P, N], F32R)
        bias = sb("bias", [P, 3 * OT], F32)
        coeff_sb = sb("coeff_sb", [P, BATCHES], F32)
        pair_ids = sb("pair_ids", [1, 3 * PAIR], I32)
        warm = sb("warm", [P, 2], F32)
        banks = [ctx.enter_context(nc.psum_tensor(f"bank{i}", [P, N], F32)) for i in range(8)]

        ids_loaded = sem("ids_loaded")
        consts_loaded = sem("consts_loaded")
        raw_loaded = [sem(f"raw_loaded{s}") for s in range(RING)]
        stage_loaded = [sem(f"stage_loaded{s}") for s in range(STAGE)]
        first_loaded = [sem(f"first_loaded{k}") for k in range(KT)]
        w2_loaded = sem("w2_loaded")
        warm_ready = sem("warm_ready")
        lora_loaded = sem("lora_loaded")
        w_hi_ready = sem("w_hi_ready")
        w_ready = sem("w_ready")
        units_done = sem("units_done")
        sign_ready = sem("sign_ready")
        merged_ready = sem("merged_ready")
        tile_done = sem("tile_done")
        tile_drained = sem("tile_drained")
        half_sum = sem("half_sum")
        act_hi_ready = sem("act_hi_ready")
        act_ready = sem("act_ready")
        lora_hi_ready = sem("lora_hi_ready")
        lora_ready = sem("lora_ready")
        h_summed = sem("h_summed")
        h_hi_ready = sem("h_hi_ready")
        h_ready = sem("h_ready")
        stored = sem("stored")
        last_stored = sem("last_stored")
        results_stored = sem("results_stored")
        ids_seen = sem("ids_seen")
        pair_entered = sem("pair_entered")
        block = ctx.enter_context(nc.Block())

        def tile(buf, o):
            return buf[:, bass.ds(o * N, N)]

        def slot(buf, s):
            return buf[:, s * UNIT:(s + 1) * UNIT]

        def stacked(b):
            return lora_a[:, b * KT * P:(b + 1) * KT * P].rearrange("p (k g r) -> p k g r", k=KT, g=STACK)

        def plain_a(b):
            return lora_a_raw[:, b * KT * RANK:(b + 1) * KT * RANK].rearrange(
                "p (k r) -> p k r", k=KT).unsqueeze(2).broadcast_to([P, KT, STACK, RANK])

        @block.sync
        def _(sp):
            def after_split(p, u):
                sp.wait_ge(w_ready, PAIR_UNITS * p + u + 1)

            def after_merge(p, u):
                sp.wait_ge(merged_ready, OWN_UNITS * p + u - RING - PHASE_UNITS + 1)

            def load_group(p, g, base, buf, free, src_of):
                for j in range(RING):
                    free(p, base + RING * g + j)
                    sp.dma_start(slot(buf, j), src_of(j)).then_inc(raw_loaded[j], 16)

            def pick(table, i):
                return table[bass.ds(i, 1), :, :].rearrange("a p n -> (a p) n")

            def load_lora(p, half, a_ids, a_table, b_table):
                sp.wait_ge(lora_ready, 2 * p + half + 1)
                for b in range(PAIR):
                    sp.dma_start(lora_a_raw[:, b * KT * RANK:(b + 1) * KT * RANK],
                                 pick(a_table, a_ids[b])).then_inc(lora_loaded, 16)
                    for g in range(2 * STACK):
                        sp.dma_start(lora_b_raw[g * RANK:(g + 1) * RANK, b * D:(b + 1) * D],
                                     pick(b_table, a_ids[b])).then_inc(lora_loaded, 16)

            def load_pair(p, last):
                sp.dma_start(pair_ids[:, :], ids[bass.ds(p, 1), :]).then_inc(ids_loaded, 16)
                sp.wait_ge(ids_loaded, 16 * (p + 1))
                sp.sem_inc(ids_seen, 1)

                def table_rows(kind, entries):
                    return [sp.value_load(pair_ids[0:1, PAIR * kind + b:PAIR * kind + b + 1],
                                          min_val=0, max_val=entries - 1) for b in range(PAIR)]

                rows = table_rows(0, w0.shape[0] // OT)
                with sp.Fori(0, OWN_GROUPS) as g:
                    load_group(p, g, 0, raw, after_split,
                               lambda j: pick(w0, rows[j % PAIR] * OT + 2 * g + j // 2))
                load_lora(p, 0, table_rows(1, a1.shape[0]), a1, lb1)
                with sp.Fori(0, OT // RING) as g:
                    load_group(p, g, OWN_UNITS, raw, after_split, lambda j: pick(w1, RING * g + j))

                def mask_unit(g):
                    return lambda j: pick(mask, (PAIR * p + j % 2) * OT + 2 * g + j // 2)

                load_group(p, 0, PHASE_UNITS, raw_mask, after_split, mask_unit(0))
                with sp.Fori(1, OWN_GROUPS) as g:
                    load_group(p, g, PHASE_UNITS, raw_mask, after_merge, mask_unit(g))
                load_lora(p, 1, table_rows(2, a3.shape[0]), a3, lb3)
                for g, free in ((0, after_merge), (1, after_split)):
                    load_group(p, g, PHASE_UNITS + OWN_UNITS, raw, free,
                               lambda j: w3[RING * g + j, :, :])
                if not last:
                    for k in range(KT):
                        sp.wait_ge(act_ready, PAIR_TILES * p + k + STAGE + 1 + (PAIR_TILES - KT) * (k >= STAGE))
                        sp.dma_start(tile(stage, k % STAGE), pick(x, (p + 1) * KT + k)).then_inc(
                            stage_loaded[k % STAGE], 16)

            with sp.Fori(0, PAIRS - 1) as p:
                load_pair(p, False)
            load_pair(PAIRS - 1, True)
            for o in range(OT):
                sp.wait_ge(tile_drained, PAIR_TILES * (PAIRS - 1) + o + DRAINED0 + 3 * OT + 1)
                sp.dma_start(out[OT * (PAIRS - 1) + o, :, :], tile(resid, o)).then_inc(last_stored, 16)
            sp.wait_ge(last_stored, 16 * OT)

        @block.gpsimd
        def _(pool):
            pool.sem_inc(results_stored, 1)
            pool.dma_start(coeff_sb[:, :], coeff).then_inc(consts_loaded, 16)
            for n, b in enumerate((b1, b2, b3)):
                pool.dma_start(bias[:, n * OT:(n + 1) * OT], b).then_inc(consts_loaded, 16)
            for o in range(OT):
                pool.wait_ge(w_ready, OWN_UNITS + o + 1)
                pool.dma_start(slot(w2_sb, o), w2[o, :, :]).then_inc(w2_loaded, 16)
            with pool.Fori(0, PAIRS - 1) as p:
                with pool.Fori(0, OT) as o:
                    pool.wait_ge(tile_drained, PAIR_TILES * p + o + DRAINED0 + 3 * OT + 1)
                    pool.dma_start(out[bass.ds(p * OT + o, 1), :, :].rearrange("a p n -> (a p) n"),
                                   tile(resid, o)).then_inc(stored, 16)
                pool.wait_ge(stored, 16 * OT * p + 16 * OT)
                pool.sem_inc(results_stored, 1)

        @block.scalar
        def _(act):
            def weight_hi(p, u, s):
                act.wait_ge(raw_loaded[s], 16 * (PAIR_GROUPS * p + 1) + 16 // RING * (u - s))
                act.wait_ge(units_done, PAIR_UNITS * p + u + 1)
                nc.scalar.activation(slot(w_hi, s), slot(raw, s), ACT.Copy).then_inc(w_hi_ready, 1)

            def sign(p, u, s):
                act.wait_ge(raw_loaded[s], 16 * (PAIR_GROUPS * p + 1) + 16 // RING * (u - s))
                nc.scalar.activation(slot(raw, s), slot(raw_mask, s), ACT.Copy,
                                     scale=2.0, bias=-1.0).then_inc(sign_ready, 1)

            def merged_hi(p, u, s):
                act.wait_ge(merged_ready, OWN_UNITS * p + u - PHASE_UNITS + 1)
                act.wait_ge(units_done, PAIR_UNITS * p + u + 1)
                nc.scalar.activation(slot(w_hi, s), slot(merged, s), ACT.Copy).then_inc(w_hi_ready, 1)

            def result_hi(p, layer, o):
                act.wait_ge(tile_drained, PAIR_TILES * p + layer * OT + o + DRAINED0 + 1)
                nc.scalar.activation(tile(act_hi[(layer + 1) % 2], o), tile(resid, o),
                                     ACT.Copy).then_inc(act_hi_ready, 1)

            def first_hi(k):
                act.wait_ge(first_loaded[k], 16)
                nc.scalar.activation(tile(act_hi[0], k), tile(resid, k), ACT.Copy).then_inc(act_hi_ready, 1)

            def next_input_hi(p, k):
                act.wait_ge(stage_loaded[k % STAGE], 16 * (KT // STAGE * p + k // STAGE + 1))
                nc.scalar.activation(tile(act_hi[0], k), tile(stage, k % STAGE), ACT.Copy).then_inc(act_hi_ready, 1)

            def lora_hi(p, half, scale):
                act.wait_ge(lora_loaded, 16 * PAIR * (1 + 2 * STACK) * (2 * p + half + 1))
                for b in range(PAIR):
                    nc.scalar.activation(stacked(b)[:, :, :, 0:RANK], plain_a(b), ACT.Copy)
                    nc.scalar.activation(lora_b[:, b * D:(b + 1) * D], lora_b_raw[:, b * D:(b + 1) * D],
                                         ACT.Copy, scale=scale).then_inc(lora_hi_ready, 1)

            def mask_tile(p, n, u, s, signs):
                merged_hi(p, u, s)
                if signs:
                    sign(p, u + RING, s)
                merged_hi(p, u + 1, s + 1)
                result_hi(p, 2, n)
                if signs:
                    sign(p, u + RING + 1, s + 1)

            def own_layer(p, layer):
                base = PHASE_UNITS * (layer // 2)
                with act.Fori(0, OWN_GROUPS - 1 - layer // 2) as g:
                    for j in range(2):
                        u = base + RING * g + RING + 2 * j
                        if layer == 2:
                            mask_tile(p, 2 * g + j, u, 2 * j, True)
                        else:
                            weight_hi(p, u, 2 * j)
                            weight_hi(p, u + 1, 2 * j + 1)
                            result_hi(p, layer, 2 * g + j)
                if layer == 2:
                    for j in range(2):
                        mask_tile(p, OT - 4 + j, base + OWN_UNITS - RING + 2 * j, 2 * j, False)
                for j in range(2):
                    u = base + OWN_UNITS + 2 * j
                    weight_hi(p, u, 2 * j)
                    result_hi(p, layer, OT - 2 + j)
                    weight_hi(p, u + 1, 2 * j + 1)

            def shared_layer(p, layer, last):
                base = PHASE_UNITS * (layer // 2) + OWN_UNITS
                half = layer // 2
                lora_hi(p, half, LORA_SCALE[layer])
                for o in range(RING):
                    if o == LORA_AFTER:
                        act.wait_ge(h_summed, 2 * p + half + 1)
                        nc.scalar.activation(lora_h[:, :], banks[LORA_BANK][:, :], ACT.Copy).then_inc(h_hi_ready, 1)
                        if layer == 1:
                            for ahead in range(RING - 1):
                                sign(p, PHASE_UNITS + ahead, ahead)
                    weight_hi(p, base + RING + o, o)
                    if layer == 3 and not last:
                        next_input_hi(p, o)
                if layer == 1:
                    for o in range(RING):
                        result_hi(p, layer, o)
                for o in range(RING, OT):
                    if layer == 1:
                        u = PHASE_UNITS + o - RING
                        sign(p, u + RING - 1, (o - 1) % RING)
                        result_hi(p, layer, o)
                        merged_hi(p, u, o % RING)
                        if o == OT - 1:
                            sign(p, u + RING, o % RING)
                    elif not last:
                        next_input_hi(p, o)
                        weight_hi(p + 1, o - RING, o % RING)

            def pair(p, last):
                own_layer(p, 0)
                shared_layer(p, 1, last)
                own_layer(p, 2)
                shared_layer(p, 3, last)

            for k in range(FIRST_AT_ONCE):
                act.dma_start(tile(resid, k), x[k, :, :]).then_inc(first_loaded[k], 16)
            act.wait_ge(warm_ready, 1)
            nc.scalar.activation(warm[:, 1:2], warm[:, 0:1], ACT.Copy)
            for k in range(FIRST_SPLIT):
                if k == 2:
                    act.wait_ge(ids_seen, 1)
                    for later in range(FIRST_AT_ONCE, KT):
                        act.dma_start(tile(resid, later), x[later, :, :]).then_inc(first_loaded[later], 16)
                first_hi(k)
            weight_hi(0, 0, 0)
            for k in range(FIRST_SPLIT, KT):
                first_hi(k)
            for u in range(1, RING):
                weight_hi(0, u, u)
            with act.Fori(0, PAIRS - 1) as p:
                pair(p, False)
            pair(PAIRS - 1, True)

        @block.vector
        def _(dve):
            def minus_hi(dst, src):
                return nc.vector.tensor_tensor(dst, src[0], src[1], ALU.subtract)

            def weight_lo(p, u, s):
                dve.wait_ge(w_hi_ready, PAIR_UNITS * p + u + 1)
                minus_hi(slot(w_lo, s), (slot(raw, s), slot(w_hi, s).bitcast(F32))).then_inc(w_ready, 1)

            def merge(p, u, s, o, b):
                dve.wait_ge(w_ready, PAIR_UNITS * p + u + 1)
                dve.wait_ge(sign_ready, OWN_UNITS * p + u - PHASE_UNITS + 1)
                nc.vector.scalar_tensor_tensor(
                    slot(merged, s), slot(raw, s), coeff_sb[:, bass.ds(PAIR * p + b, 1)],
                    w2_sb[:, bass.ds(o * UNIT, UNIT)], ALU.mult, ALU.add).then_inc(merged_ready, 1)

            def merged_lo(p, u, s):
                dve.wait_ge(w_hi_ready, PAIR_UNITS * p + u + 1)
                minus_hi(slot(w_lo, s), (slot(merged, s), slot(w_hi, s).bitcast(F32))).then_inc(w_ready, 1)

            def sum_tile(p, layer, o, bank):
                if layer % 2:
                    dve.wait_ge(tile_done, PHASE_TILES * p + layer // 2 * OT + o + 1)
                else:
                    dve.wait_ge(units_done, RING + PAIR_UNITS * p + layer // 2 * PHASE_UNITS + PAIR * (o + 1))
                if layer == 0:
                    nc.vector.tensor_tensor(tile(resid, o), banks[bank][:, :], tile(act_hi[0], o).bitcast(F32),
                                            ALU.add).then_inc(half_sum, 1)
                    dve.wait_ge(half_sum, OT * p + o + 1)
                    nc.vector.tensor_tensor(tile(resid, o), tile(resid, o), tile(act_lo[0], o).bitcast(F32),
                                            ALU.add).then_inc(tile_drained, 1)
                else:
                    nc.vector.scalar_tensor_tensor(
                        tile(resid, o), banks[bank][:, :], bias[:, bass.ds((layer - 1) * OT + o, 1)],
                        tile(resid, o), ALU.add, ALU.add).then_inc(tile_drained, 1)

            def result_lo(p, layer, o):
                dve.wait_ge(act_hi_ready, PAIR_TILES * p + (layer + 1) * OT + o + 1)
                s = (layer + 1) % 2
                minus_hi(tile(act_lo[s], o),
                         (tile(resid, o), tile(act_hi[s], o).bitcast(F32))).then_inc(act_ready, 1)

            def input_lo(p, k, src):
                dve.wait_ge(act_hi_ready, PAIR_TILES * p + k + 1)
                minus_hi(tile(act_lo[0], k), (src, tile(act_hi[0], k).bitcast(F32))).then_inc(act_ready, 1)

            def lora_lo(p, half, scale):
                for b in range(PAIR):
                    dve.wait_ge(lora_hi_ready, PAIR * (2 * p + half) + b + 1)
                    hi = stacked(b)[:, :, :, 0:RANK].bitcast(F32)
                    minus_hi(stacked(b)[:, :, :, RANK:2 * RANK], (plain_a(b), hi))
                    low = lora_b[P // 2:P, b * D:(b + 1) * D]
                    last = nc.vector.scalar_tensor_tensor(low, lora_b_raw[P // 2:P, b * D:(b + 1) * D], scale,
                                                          low.bitcast(F32), ALU.mult, ALU.subtract)
                last.then_inc(lora_ready, 1)

            def h_lo(p, half):
                dve.wait_ge(h_hi_ready, 2 * p + half + 1)
                for q in (P // 4, 3 * P // 4):
                    rows = slice(q, q + P // 4)
                    last = nc.vector.tensor_tensor(lora_h[rows, :], banks[LORA_BANK][rows, :],
                                                   lora_h[rows, :].bitcast(F32), ALU.subtract)
                last.then_inc(h_ready, 1)

            def plain_tile(p, n, u, s, bank):
                weight_lo(p, u, s)
                sum_tile(p, 0, n, bank)
                weight_lo(p, u + 1, s + 1)
                result_lo(p, 0, n)

            def mask_tile(p, n, u, s, bank, merges):
                merged_lo(p, u, s)
                sum_tile(p, 2, n, bank)
                if merges:
                    merge(p, u + RING, s, n + 4, 0)
                merged_lo(p, u + 1, s + 1)
                result_lo(p, 2, n)
                if merges:
                    merge(p, u + RING + 1, s + 1, n + 4, 1)

            def own_layer(p, layer):
                base = PHASE_UNITS * (layer // 2)
                with dve.Fori(0, OWN_GROUPS - 1 - layer // 2) as g:
                    for j in range(2):
                        u = base + RING * g + RING + 2 * j
                        if layer == 2:
                            mask_tile(p, 2 * g + j, u, 2 * j, j, True)
                        else:
                            plain_tile(p, 2 * g + j, u, 2 * j, j)
                if layer == 2:
                    for j in range(2):
                        mask_tile(p, OT - 4 + j, base + OWN_UNITS - RING + 2 * j, 2 * j, j, False)
                for j in range(2):
                    u = base + OWN_UNITS + 2 * j
                    weight_lo(p, u, 2 * j)
                    sum_tile(p, layer, OT - 2 + j, j)
                    result_lo(p, layer, OT - 2 + j)
                    weight_lo(p, u + 1, 2 * j + 1)

            def shared_layer(p, layer, last):
                base = PHASE_UNITS * (layer // 2) + OWN_UNITS
                half = layer // 2
                lora_lo(p, half, LORA_SCALE[layer])
                for o in range(RING):
                    if o == LORA_AFTER:
                        h_lo(p, half)
                        if layer == 1:
                            dve.wait_ge(w2_loaded, 16 * OT)
                            for ahead in range(RING - 1):
                                merge(p, PHASE_UNITS + ahead, ahead, ahead // PAIR, ahead % PAIR)
                    weight_lo(p, base + RING + o, o)
                    if layer == 3 and not last:
                        input_lo(p + 1, o, tile(stage, o))
                for o in range(RING):
                    sum_tile(p, layer, o, SHARED_BANK[o])
                    if layer == 1 and o:
                        result_lo(p, layer, o - 1)
                if layer == 1:
                    result_lo(p, layer, RING - 1)
                for o in range(RING, OT):
                    if layer == 1:
                        u = PHASE_UNITS + o - RING
                        sum_tile(p, layer, o, SHARED_BANK[o])
                        merge(p, u + RING - 1, (o - 1) % RING, (o - 1) // PAIR, (o - 1) % PAIR)
                        result_lo(p, layer, o)
                        merged_lo(p, u, o % RING)
                        if o == OT - 1:
                            merge(p, u + RING, o % RING, o // PAIR, o % PAIR)
                    else:
                        if not last:
                            input_lo(p + 1, o, tile(stage, o % STAGE))
                        sum_tile(p, layer, o, SHARED_BANK[o])
                        if not last:
                            weight_lo(p + 1, o - RING, o % RING)

            def pair(p, last):
                dve.wait_ge(results_stored, p + 1)
                dve.sem_inc(pair_entered, 1)
                dve.wait_ge(consts_loaded, 4 * 16)
                own_layer(p, 0)
                shared_layer(p, 1, last)
                own_layer(p, 2)
                shared_layer(p, 3, last)

            nc.vector.memset(warm[:, 0:1], 0.0).then_inc(warm_ready, 1)
            dve.sem_inc(w_ready, RING)
            dve.sem_inc(tile_drained, DRAINED0)
            dve.sem_inc(lora_ready, 1)
            for k in range(FIRST_SPLIT):
                input_lo(0, k, tile(resid, k))
            weight_lo(0, 0, 0)
            for k in range(FIRST_SPLIT, KT):
                input_lo(0, k, tile(resid, k))
            for u in range(1, RING):
                weight_lo(0, u, u)
            with dve.Fori(0, PAIRS - 1) as p:
                pair(p, False)
            pair(PAIRS - 1, True)

        @block.tensor
        def _(pe):
            def products(s, out_ap, cols, src, ks, close=True, k_wait=None):
                for k in ks:
                    if k_wait is not None:
                        pe.wait_ge(act_ready, k_wait + k + 1)
                    hi = w_hi[:, s * UNIT + k * P:s * UNIT + (k + 1) * P]
                    lo = w_lo[:, s * UNIT + k * P:s * UNIT + (k + 1) * P]
                    x_hi = act_hi[src][:, k * N + cols.start:k * N + cols.stop]
                    x_lo = act_lo[src][:, k * N + cols.start:k * N + cols.stop]
                    nc.tensor.matmul(out_ap, hi, x_hi, start=(k == 0), stop=False)
                    nc.tensor.matmul(out_ap, hi, x_lo, start=False, stop=False)
                    last = nc.tensor.matmul(out_ap, lo, x_hi, start=False, stop=(close and k == KT - 1))
                return last

            batch_cols = [slice(b * TOKENS, (b + 1) * TOKENS) for b in range(PAIR)]

            def bank_drained(f, g, j):
                pe.wait_ge(tile_drained, PHASE_TILES * f + 2 * g + j + 1)

            def unit_split(f, u):
                pe.wait_ge(w_ready, RING + PHASE_UNITS * f + u + 1)

            def own_group(f, g):
                for j in range(2):
                    bank_drained(f, g, j)
                    for b in range(PAIR):
                        s = PAIR * j + b
                        unit_split(f, RING * g + s)
                        products(s, banks[j][:, batch_cols[b]], batch_cols[b], 0, range(KT)).then_inc(units_done, 1)

            def own_first_group(f):
                def unit(s, ks, close=True, k_wait=None):
                    return products(s, banks[s // PAIR][:, batch_cols[s % PAIR]], batch_cols[s % PAIR], 0,
                                    ks, close, k_wait)

                bank_drained(f, 0, 0)
                unit_split(f, 0)
                unit(0, range(KT - 1), False, PHASE_TILES * f)
                bank_drained(f, 0, 1)
                unit_split(f, 2)
                unit(2, range(KT // 2), False)
                unit(0, range(KT - 1, KT), True, PHASE_TILES * f).then_inc(units_done, 1)
                unit(1, range(KT)).then_inc(units_done, 1)
                unit(2, range(KT // 2, KT)).then_inc(units_done, 1)
                unit_split(f, 3)
                unit(3, range(KT)).then_inc(units_done, 1)

            def low_rank(f):
                pe.wait_ge(lora_ready, f + 2)
                for b in range(PAIR):
                    cols = slice(b * TOKENS, (b + 1) * TOKENS)
                    for k in range(KT):
                        a = lora_a[:, (b * KT + k) * P:(b * KT + k + 1) * P]
                        for i, part in enumerate((act_hi[1], act_lo[1])):
                            last = nc.tensor.matmul(
                                banks[LORA_BANK][:, cols], a,
                                part[:, k * N + b * TOKENS:k * N + (b + 1) * TOKENS],
                                start=(k == 0 and i == 0), stop=(k == KT - 1 and i == 1))
                last.then_inc(h_summed, 1)

            def low_rank_out(o):
                for b in range(PAIR):
                    cols = slice(b * TOKENS, (b + 1) * TOKENS)
                    last = nc.tensor.matmul(banks[SHARED_BANK[o]][:, cols],
                                            lora_b[:, b * D + o * P:b * D + (o + 1) * P], lora_h[:, cols],
                                            start=False, stop=(b == PAIR - 1))
                last.then_inc(tile_done, 1)

            def shared_tile(o, ks, close=False, k_wait=None):
                return products(o % RING, banks[SHARED_BANK[o]][:, :], slice(0, N), 1, ks, close, k_wait)

            pe.sem_inc(units_done, RING)
            with pe.Fori(0, PHASES) as f:
                own_first_group(f)
                with pe.Fori(1, OWN_GROUPS) as g:
                    own_group(f, g)
                unit_split(f, OWN_UNITS)
                shared_tile(0, range(KT - 1), k_wait=PHASE_TILES * f + OT)
                unit_split(f, OWN_UNITS + 1)
                shared_tile(1, range(KT // 2))
                shared_tile(0, range(KT - 1, KT), k_wait=PHASE_TILES * f + OT).then_inc(units_done, 1)
                shared_tile(1, range(KT // 2, KT)).then_inc(units_done, 1)
                for o in range(2, OT):
                    if o == LORA_AFTER:
                        low_rank(f)
                    if SHARED_BANK[o] < OWN_BANKS or o == OT - 1:
                        before = OT - OWN_BANKS + SHARED_BANK[o] if o < OT - 1 else OT
                        pe.wait_ge(tile_drained, PHASE_TILES * f + before + DRAINED0 + 1)
                    unit_split(f, OWN_UNITS + o)
                    shared_tile(o, range(KT)).then_inc(units_done, 1)
                    if o == LORA_AFTER:
                        pe.wait_ge(h_ready, f + 1)
                        for done in range(o):
                            low_rank_out(done)
                    if o >= LORA_AFTER:
                        low_rank_out(o)


def kernel(x, itok_B_3_7, itok_B_0_23, condB_coeff, itok_B_6_15, mask_Bx4096x4096_ik1, L0_cond_weight,
           L1_cond_W, L1_cond_b, L1_cond_lora_As, L1_cond_lora_Bs, L2_cond_W, L2_cond_b,
           L3_cond_base_weight, L3_cond_base_bias, L3_cond_lora_A_w, L3_cond_lora_B_w):
    import numpy as np
    import concourse.bacc as bacc
    from concourse.bass_utils import run_bass_kernel_spmd as run

    def units(w):
        w = np.asarray(w).reshape(-1, OT, P, KT, P)
        return np.ascontiguousarray(w.transpose(0, 1, 4, 3, 2)).reshape(-1, P, UNIT)

    m = np.asarray(mask_Bx4096x4096_ik1).reshape(BATCHES, KT, P, OT, P)
    ids = np.stack([np.asarray(i).reshape(PAIRS, PAIR) for i in (itok_B_3_7, itok_B_0_23, itok_B_6_15)], axis=1)
    a3 = np.asarray(L3_cond_lora_A_w)
    arrays = {
        "x": np.asarray(x).reshape(PAIRS, PAIR, TOKENS, KT, P).transpose(0, 3, 4, 1, 2).reshape(PAIRS * KT, P, N),
        "ids": ids.reshape(PAIRS, 3 * PAIR),
        "coeff": np.asarray(condB_coeff).reshape(1, BATCHES),
        "w0": units(L0_cond_weight),
        "w1": units(L1_cond_W),
        "w2": units(L2_cond_W),
        "w3": units(L3_cond_base_weight),
        "mask": m.transpose(0, 3, 2, 1, 4).reshape(BATCHES * OT, P, UNIT),
        "b1": np.asarray(L1_cond_b).reshape(OT, P).T,
        "b2": np.asarray(L2_cond_b).reshape(OT, P).T,
        "b3": np.asarray(L3_cond_base_bias).reshape(OT, P).T,
        "a1": np.asarray(L1_cond_lora_As).reshape(-1, KT, P, RANK).transpose(0, 2, 1, 3).reshape(-1, P, KT * RANK),
        "a3": a3.reshape(-1, RANK, KT, P).transpose(0, 3, 2, 1).reshape(-1, P, KT * RANK),
        "lb1": np.asarray(L1_cond_lora_Bs),
        "lb3": np.asarray(L3_cond_lora_B_w).transpose(0, 2, 1),
    }
    arrays = {f"{k}_dram": np.ascontiguousarray(v) for k, v in arrays.items()}
    nc = bacc.Bacc("TRN2", target_bir_lowering=False, num_devices=1)
    args = {k[:-5]: nc.dram_tensor(k, v.shape, mybir.dt.from_np(v.dtype), kind="ExternalInput").ap()
            for k, v in arrays.items()}
    args["coeff"] = args["coeff"].broadcast_to([P, BATCHES])
    out = nc.dram_tensor("out_dram", (PAIRS * OT, P, N), F32, kind="ExternalOutput").ap()
    build(nc, out=out, **args)
    r = run(nc, [arrays], core_ids=[0])
    y = np.asarray(r.results[0]["out_dram"]).reshape(PAIRS, OT, P, PAIR, TOKENS)
    return y.transpose(0, 3, 4, 1, 2).reshape(BATCHES, TOKENS, D)
```
